# Optimizing a Trainium2 kernel written in Bass

```python
import numpy as np
import jax
import jax.numpy as jnp

def _softmax(x, axis=-1):
    return jax.nn.softmax(x, axis=axis)

def _gelu(x):
    return jax.nn.gelu(x, approximate=True)

def _silu(x):
    return jax.nn.silu(x)

def _sigmoid(x):
    return jax.nn.sigmoid(x)

def _layernorm(x, axis=-1, eps=1e-05):
    m = jnp.mean(x, axis=axis, keepdims=True)
    v = jnp.var(x, axis=axis, keepdims=True)
    return (x - m) / jnp.sqrt(v + eps)

def _scatter_add(tgt, idx, src, axis=0):
    return tgt.at[idx].add(src)

def _segment_sum(src, seg, n):
    return jax.ops.segment_sum(src, seg, n)
kernel_name = 'mk_rec_standalone_d1_rec_r8_2362e5'

def setup_inputs(seed: int=0):
    np.random.seed(seed)
    _w = jnp.asarray

    def _rec_inputs():
        import jax
        import jax.numpy as jnp
        _rk = jax.random.key(seed)
        r_x = 8.71811e-05 + 1.00005 * jax.random.normal(jax.random.fold_in(_rk, 1), (512, 39, 16), jnp.float32)
        return r_x
    r_x = _rec_inputs()

    def _L0_rec_setup():
        import jax, jax.numpy as jnp
        import numpy as np
        B, F, D = (1024, 39, 16)
        HIDDEN = [128, 128, 128]

        def _cin(x, Ws, bs):
            F0 = x.shape[1]
            h = x
            outs = []
            n = len(Ws)
            for i, (W, b) in enumerate(zip(Ws, bs)):
                L = W.shape[-1]
                Fk = h.shape[1]
                Wr = W.reshape(F0, Fk, L)
                z = jnp.einsum('bfd,bgd->bfgd', x, h)
                cur = jax.nn.relu(jnp.einsum('bfgd,fgl->bld', z, Wr) + b[None, :, None])
                if i != n - 1:
                    h = cur[:, :L // 2]
                    direct = cur[:, L // 2:]
                else:
                    direct = cur
                outs.append(direct)
            return jnp.concatenate(outs, axis=1).sum(-1)
        key = jax.random.key(seed)
        ks = jax.random.split(key, 8)
        x = jax.random.normal(ks[0], (B, F, D), dtype=jnp.float32)
        field_nums = [F]
        Ws, bs = ([], [])
        for i, L in enumerate(HIDDEN):
            fan_in = field_nums[0] * field_nums[-1]
            lim = np.sqrt(6.0 / fan_in)
            Ws.append(jax.random.uniform(ks[1 + i], (fan_in, L), jnp.float32, -lim, lim))
            bs.append(jnp.zeros((L,), jnp.float32))
            field_nums.append(L // 2)
        return {'x': x, 'W0': Ws[0], 'W1': Ws[1], 'W2': Ws[2], 'b0': bs[0], 'b1': bs[1], 'b2': bs[2]}
    _L0_rec_all = _L0_rec_setup()
    _L0_rec_in = {k: v for k, v in _L0_rec_all.items() if k in ('W0', 'W1', 'W2', 'b0', 'b1', 'b2')}
    del _L0_rec_all
    return {'r_x': r_x, 'L0_rec_W0': _L0_rec_in['W0'], 'L0_rec_W1': _L0_rec_in['W1'], 'L0_rec_W2': _L0_rec_in['W2'], 'L0_rec_b0': _L0_rec_in['b0'], 'L0_rec_b1': _L0_rec_in['b1'], 'L0_rec_b2': _L0_rec_in['b2']}

def reference(r_x, L0_rec_W0, L0_rec_W1, L0_rec_W2, L0_rec_b0, L0_rec_b1, L0_rec_b2):
    import jax
    import jax.numpy as jnp

    def _L0_rec_ref(x, W0, W1, W2, b0, b1, b2):
        import jax, jax.numpy as jnp
        import numpy as np
        B, F, D = (1024, 39, 16)
        HIDDEN = [128, 128, 128]

        def _cin(x, Ws, bs):
            F0 = x.shape[1]
            h = x
            outs = []
            n = len(Ws)
            for i, (W, b) in enumerate(zip(Ws, bs)):
                L = W.shape[-1]
                Fk = h.shape[1]
                Wr = W.reshape(F0, Fk, L)
                z = jnp.einsum('bfd,bgd->bfgd', x, h)
                cur = jax.nn.relu(jnp.einsum('bfgd,fgl->bld', z, Wr) + b[None, :, None])
                if i != n - 1:
                    h = cur[:, :L // 2]
                    direct = cur[:, L // 2:]
                else:
                    direct = cur
                outs.append(direct)
            return jnp.concatenate(outs, axis=1).sum(-1)
        return _cin(x, [W0, W1, W2], [b0, b1, b2])
    y = _L0_rec_ref(r_x, L0_rec_W0, L0_rec_W1, L0_rec_W2, L0_rec_b0, L0_rec_b1, L0_rec_b2)
    return y

_drawn_inputs = setup_inputs


def setup_inputs(seed=0):
    import zlib

    import numpy as np

    out = dict(_drawn_inputs(seed))
    spreads = {'L0_rec_b0': (0.0, 0.1), 'L0_rec_b1': (0.0, 0.1), 'L0_rec_b2': (0.0, 0.1)}
    factors = {}
    for name, (base, spread) in spreads.items():
        noise = np.random.default_rng([zlib.crc32(name.encode()), seed]).standard_normal(out[name].shape)
        drawn = base * np.exp(spread * noise) if base else spread * noise
        out[name] = jnp.asarray(drawn.astype(out[name].dtype))
    for name, factor in factors.items():
        out[name] = (out[name] * factor).astype(out[name].dtype)
    return out
```

```python
from contextlib import ExitStack

import concourse.bass as bass
from concourse import mybir

F32 = mybir.dt.float32
F32R = mybir.dt.float32r
ALU = mybir.AluOpType
ACT = mybir.ActivationFunctionType

P = 128
B = 512
D = 16
F = 39
L = 128
H = L // 2
GROUP = 2
XLOAD = 2
SHIFTS = F // 2 + 1
TILES = {0: 7, 1: 20, 2: 20}
RING = 8
LAG = 6
PAIR_ROWS = 3 * F

VV, PP, PN, N = (2, 0, 0), (0, 2, 0), (0, 1, 1), (0, 0, 1)
MIX = {0: [VV, PN, PP, N],
       1: [VV, PN, PP, PN, VV, PN, PP, PN, PP, PN],
       2: [PP, PN, VV, PN, PP, PN, VV, PN, PP, PN]}

TAIL = 6
STEPS = ([(1, g, 0) for g in range(10)] + [(2, g, -1) for g in range(TAIL, 10)]
         + [(0, g, 1) for g in range(4)] + [(2, g, 0) for g in range(TAIL)])
STEP = {(layer, g): s for s, (layer, g, _) in enumerate(STEPS)}
A_LAST, B_LAST, C_LAST = STEP[1, 9], STEP[2, 9], STEP[0, 3]
STEADY = 1
assert len(STEPS) % RING == 0


def steps_of(i):
    if not isinstance(i, int):
        return list(range(len(STEPS)))
    return [s for s, (_, _, off) in enumerate(STEPS) if 0 <= i + off < D]


def tally(counts):
    total, at = 0, {}
    for i in range(-1, D + 1):
        for s in steps_of(i):
            total += counts(*MIX[STEPS[s][0]][STEPS[s][1]])
            at[i, s] = total
    each = sum(counts(*MIX[layer][g]) for layer, g, _ in STEPS)

    def after(i, s):
        if isinstance(i, int):
            return at[i, s]
        return (i - STEADY) * each + at[STEADY, s]
    return after


groups_over = tally(lambda v, p, n: 1)
vect_over = tally(lambda v, p, n: int(v > 0))
pool_over = tally(lambda v, p, n: int(p > 0))
rounded_over = tally(lambda v, p, n: int(v + p > 0))


def slot_of(i, s):
    return (groups_over(i if isinstance(i, int) else STEADY, s) - 1) % RING


def zh_at(slot):
    return slot // 2 * 3 + slot % 2 * 2


def tiles_of(layer, g):
    return min(GROUP, TILES[layer] - GROUP * g)


SPLIT, NATIVE = {}, {}
for _layer in (0, 1, 2):
    for _t in range(TILES[_layer]):
        _v, _p, _n = MIX[_layer][_t // GROUP]
        assert _v + _p + _n == tiles_of(_layer, _t // GROUP) and _v + _p <= 2 - STEP[_layer, _t // GROUP] % 2
        _to = SPLIT if _t % GROUP < _v + _p else NATIVE
        _to[_layer, _t] = len(_to)


SPLIT_GROUPS = {layer: sum(v + p > 0 for v, p, _ in MIX[layer]) for layer in MIX}


def cin_kernel(nc, x, w0a, w0b, w1, w2, b0, b1, b2, ident_in, out):
    with ExitStack() as ctx:
        def sb(name, shape, dt):
            return ctx.enter_context(nc.sbuf_tensor(name, shape, dt))

        def pb(name, shape):
            return ctx.enter_context(nc.psum_tensor(name, shape, F32))

        def sem(name):
            return ctx.enter_context(nc.semaphore(name))

        xb = [sb(f"xb{k}", [P, TILES[1], B], F32) for k in range(2)]
        xr = sb("xr", [P, TILES[0], B], F32)
        x3 = sb("x3", [P, B], F32)
        with nc.sbuf_tensor("z", [P, RING, GROUP, B], F32) as z:
            pass
        zl = sb("zl", [P, RING, GROUP, B], F32R)
        zh = sb("zh", [P, RING // 2 * 3, B], F32R)
        wh = sb("wh", [P, len(SPLIT), L], F32R)
        wl = sb("wl", [P, len(SPLIT), L], F32R)
        wn = sb("wn", [P, len(NATIVE), L], F32)
        direct01 = sb("direct01", [P, B], F32)
        direct2 = sb("direct2", [P, B], F32)
        sum01 = sb("sum01", [P, B], F32)
        sum2 = sb("sum2", [P, B], F32)
        bias = sb("bias", [P, 3], F32)
        ident = sb("ident", [P, P], F32)

        acc = {n: pb(f"acc{n}", [P, B]) for n in (0, 1, 2)}
        h = {1: pb("h_in1", [P, B]), 2: pb("h_in2", [P, B]), 0: pb("x3p", [P, B])}
        zv = pb("zv", [P, 2, B])

        stage = xb[1][:].rearrange("p t (a l) -> p (t a) l", l=L)
        stage_at = {0: 2 * TILES[0], 1: 3 * TILES[0], 2: 3 * TILES[0] + TILES[1]}

        x_in = [[sem(f"x_in{k}_{g}") for g in range(5)] for k in range(2)]
        xr_in = [sem(f"xr_in{g}") for g in range(2)]
        x3_in = sem("x3_in")
        x3_ready = sem("x3_ready")
        w0_in, w_in = sem("w0_in"), {1: sem("w1_in"), 2: sem("w2_in")}
        small_in, wn_in = sem("small_in"), sem("wn_in")
        w0_folded, w0_native = sem("w0_folded"), sem("w0_native")
        w_rounded, w_split = sem("w_rounded"), {n: sem(f"w{n}_split") for n in (0, 1, 2)}
        z_made = sem("z_made")
        zh_ready = sem("zh_ready")
        vect_split, pool_split = sem("vect_split"), sem("pool_split")
        group_used = sem("group_used")
        h_ready = {1: sem("h1_ready"), 2: sem("h2_ready")}
        acc_read = {n: sem(f"acc{n}_read") for n in (0, 1, 2)}
        sums_zero = sem("sums_zero")
        added01, added2 = sem("added01"), sem("added2")
        turned, out_ready, out_done = sem("turned"), sem("out_ready"), sem("out_done")

        def rows(layer):
            return PAIR_ROWS if layer == 0 else P

        block = ctx.enter_context(nc.Block())

        @block.sync
        def _(sp):
            wide = XLOAD * GROUP
            x_loads = TILES[1] // wide

            def load_x(chunk, par, q):
                for half in range(2):
                    src = x[chunk, 2 * wide * q + half, :]
                    src = bass.AP(tensor=src.tensor, offset=src.offset, ap=[[0, H], [2 * B, wide], [1, B]])
                    sp.dma_start(xb[par][half * H:(half + 1) * H, wide * q:wide * (q + 1), :],
                                 src).then_inc(x_in[par][q], 16)

            def load_shifted(chunk, q):
                t0, n = wide * q, min(wide, TILES[0] - wide * q)
                for j in range(3):
                    src = x[chunk, 3 * t0 + j, :]
                    src = bass.AP(tensor=src.tensor, offset=src.offset, ap=[[B, F], [3 * B, n], [1, B]])
                    sp.dma_start(xr[j * F:(j + 1) * F, t0:t0 + n, :], src).then_inc(xr_in[q], 16)

            def load_x3(chunk):
                for j in range(3):
                    sp.dma_start(x3[j * F:(j + 1) * F, :], x[chunk, 0:F, :]).then_inc(x3_in, 16)

            def iteration(i, par):
                first, last = (i == 0, i == D - 2) if isinstance(i, int) else (False, False)
                if not last:
                    sp.wait_ge(x3_ready, i + 2)
                    load_x3(i + 2)
                for q in range(x_loads):
                    g = XLOAD * q + XLOAD - 1
                    if g < TAIL and first:
                        sp.wait_ge(w_split[1], SPLIT_GROUPS[1])
                        sp.wait_ge(w_split[2], SPLIT_GROUPS[2])
                    elif g < TAIL:
                        sp.wait_ge(z_made, groups_over(i - 1, STEP[2, g]))
                    elif not first:
                        sp.wait_ge(z_made, groups_over(i, STEP[2, g]))
                    load_x(i + 1, 1 - par, q)
                if not last:
                    for q in range(2):
                        sp.wait_ge(z_made, groups_over(i, STEP[0, XLOAD * q + 1]))
                        load_shifted(i + 2, q)

            load_x3(0)
            for q in range(2):
                load_shifted(0, q)
            for q in range(x_loads):
                load_x(0, 0, q)
            for q in range(2):
                sp.wait_ge(z_made, groups_over(-1, STEP[0, XLOAD * q + 1]))
                load_shifted(1, q)
            sp.wait_ge(x3_ready, 1)
            load_x3(1)
            iteration(0, 0)
            with sp.Fori(0, (D - 4) // 2) as pair:
                iteration(2 * pair + 1, 1)
                iteration(2 * pair + 2, 0)
            iteration(D - 3, 1)
            iteration(D - 2, 0)
            sp.wait_ge(out_ready, 2)
            sp.dma_start(out.rearrange("(k p) c -> p k c", p=P),
                         z[:, 0, 0:2, :].rearrange("p a (k c) -> p (a k) c", c=2 * L)).then_inc(out_done, 16)
            sp.wait_ge(out_done, 16)

        @block.vector
        def _(dve):
            def split_weights(layer):
                for g, (v, p, _) in enumerate(MIX[layer]):
                    if v + p:
                        at = SPLIT[layer, GROUP * g]
                        s0 = stage_at[layer] + GROUP * g
                        dve.tensor_tensor(wl[:, at:at + v + p, :], stage[:, s0:s0 + v + p, :],
                                          wh[:, at:at + v + p, :].bitcast(F32), ALU.subtract).then_inc(w_split[layer], 1)

            def make(i, s, par):
                layer, g, off = STEPS[s]
                v, _, _ = MIX[layer][g]
                rw, n, slot = rows(layer), tiles_of(layer, g), slot_of(i, s)
                over = groups_over(i, s)
                if layer == 0:
                    dve.wait_ge(xr_in[g // XLOAD], 48 * (i + 2))
                    if g == 0:
                        dve.wait_ge(x3_ready, i + 2)
                else:
                    nth = (i + off) // 2 if isinstance(i, int) else (i + off - (par + off) % 2) // 2
                    dve.wait_ge(x_in[(par + off) % 2][g // XLOAD], 32 * (nth + 1))
                    if g == 0:
                        dve.wait_ge(h_ready[layer], 2 * (i + 1))
                if v:
                    if not (isinstance(i, int) and vect_over(i, s) == 1):
                        dve.wait_ge(vect_split, vect_over(i, s) - 1)
                    to = zv[0:rw, 0:n, :]
                else:
                    if not (isinstance(i, int) and over <= RING):
                        dve.wait_ge(group_used, over - RING)
                    to = z[0:rw, slot, 0:n, :]
                t0 = GROUP * g
                xs = xr if layer == 0 else xb[(par + off) % 2]
                dve.tensor_tensor(to, xs[0:rw, t0:t0 + n, :], h[layer][0:rw, :].unsqueeze(1).to_broadcast([rw, n, B]),
                                  ALU.mult).then_inc(z_made, 1)

            def split(i, s):
                rw, slot = rows(STEPS[s][0]), slot_of(i, s)
                dve.wait_ge(zh_ready, rounded_over(i, s))
                dve.tensor_tensor(zl[0:rw, slot, :, :], zv[0:rw, :, :],
                                  zh[0:rw, zh_at(slot):zh_at(slot) + 2, :].bitcast(F32),
                                  ALU.subtract).then_inc(vect_split, 1)

            def iteration(i, par):
                waiting = None
                for s in steps_of(i):
                    make(i, s, par)
                    if waiting is not None:
                        split(i, waiting)
                    layer, g, _ = STEPS[s]
                    waiting = s if MIX[layer][g][0] else None
                assert waiting is None

            dve.memset(sum01[:], 0.0).then_inc(sums_zero, 1)
            dve.memset(sum2[:], 0.0).then_inc(sums_zero, 1)
            dve.wait_ge(w0_in, 32)
            folded = stage_at[0]
            dve.tensor_tensor(stage[:, folded:folded + TILES[0], :], stage[:, 0:TILES[0], :],
                              stage[:, TILES[0]:2 * TILES[0], :], ALU.add).then_inc(w0_folded, 1)
            dve.wait_ge(w0_folded, 1)
            for (layer, t), at in NATIVE.items():
                if layer == 0:
                    dve.tensor_copy(wn[:, at, :], stage[:, folded + t, :]).then_inc(w0_native, 1)
            dve.wait_ge(w_rounded, SPLIT_GROUPS[0])
            split_weights(0)
            iteration(-1, 1)
            dve.wait_ge(w_rounded, SPLIT_GROUPS[0] + SPLIT_GROUPS[1])
            split_weights(1)
            iteration(0, 0)
            with dve.Fori(0, (D - 4) // 2) as pair:
                iteration(2 * pair + 1, 1)
                iteration(2 * pair + 2, 0)
            iteration(D - 3, 1)
            iteration(D - 2, 0)
            iteration(D - 1, 1)
            iteration(D, 0)
            dve.wait_ge(turned, 1)
            dve.tensor_copy(z[:, 0, 0:2, :].rearrange("p a (k c) -> p (a k) c", c=2 * L)[:, :, 0:L],
                            acc[1][:].rearrange("p (k c) -> p k c", c=L)).then_inc(out_ready, 1)

        @block.scalar
        def _(act):
            def round_weights(layer):
                for g, (v, p, _) in enumerate(MIX[layer]):
                    if v + p:
                        at = SPLIT[layer, GROUP * g]
                        s0 = stage_at[layer] + GROUP * g
                        act.activation(wh[:, at:at + v + p, :], stage[:, s0:s0 + v + p, :], ACT.Copy).then_inc(w_rounded, 1)

            def round_products(i, s):
                layer, g, _ = STEPS[s]
                v, p, _ = MIX[layer][g]
                rw, slot, k = rows(layer), slot_of(i, s), v + p
                if k == 0:
                    return
                if not (isinstance(i, int) and groups_over(i, s) <= RING):
                    act.wait_ge(group_used, groups_over(i, s) - RING)
                act.wait_ge(z_made, groups_over(i, s))
                src = zv[0:rw, 0:k, :] if v else z[0:rw, slot, 0:k, :]
                act.activation(zh[0:rw, zh_at(slot):zh_at(slot) + k, :], src, ACT.Copy).then_inc(zh_ready, 1)

            def relu_out(layer, i, h_free, group, direct):
                act.wait_ge(group_used, group)
                if layer == 1 and not (isinstance(i, int) and i < 1):
                    act.wait_ge(added01, i)
                if h_free is not None:
                    act.wait_ge(z_made, h_free)
                for half in range(2):
                    act.activation(h[layer + 1][half * H:(half + 1) * H, :], acc[layer][0:H, :], ACT.Relu,
                                   bias=bias[0:H, layer:layer + 1]).then_inc(h_ready[layer + 1], 1)
                act.activation(direct, acc[layer][H:L, :], ACT.Relu,
                               bias=bias[H:L, layer:layer + 1]).then_inc(acc_read[layer], 1)

            def relu_last(i):
                act.wait_ge(group_used, groups_over(i, B_LAST))
                if not (isinstance(i, int) and i < 2):
                    act.wait_ge(added2, i - 1)
                act.activation(direct2[:], acc[2][:], ACT.Relu, bias=bias[:, 2:3]).then_inc(acc_read[2], 1)

            def copy_x3(i, g_done):
                act.wait_ge(x3_in, 48 * (i + 3))
                if g_done is not None:
                    act.wait_ge(z_made, g_done)
                act.activation(h[0][0:PAIR_ROWS, :], x3[0:PAIR_ROWS, :], ACT.Copy).then_inc(x3_ready, 1)

            def iteration(i, par):
                number = isinstance(i, int)
                for s in steps_of(i):
                    if s == A_LAST + LAG or (number and i == D - 1 and s == STEP[2, 0]):
                        relu_out(1, i, None if number and i < 1 else groups_over(i, B_LAST),
                                 groups_over(i, A_LAST), direct01[H:L, :])
                    if s == B_LAST + LAG and not (number and i < 1):
                        relu_last(i)
                    if s == C_LAST + LAG and not (number and i > D - 2):
                        relu_out(0, i, groups_over(i, A_LAST), groups_over(i, C_LAST), direct01[0:H, :])
                    round_products(i, s)
                    if s == C_LAST and not (number and i >= D - 2):
                        copy_x3(i, groups_over(i, C_LAST))

            act.dma_start(stage[:, 0:TILES[0], :], w0a).then_inc(w0_in, 16)
            act.dma_start(stage[:, TILES[0]:2 * TILES[0], :], w0b).then_inc(w0_in, 16)
            for n, b in enumerate((b0, b1, b2)):
                act.dma_start(bias[:, n:n + 1], b.rearrange("(l a) -> l a", a=1)).then_inc(small_in, 16)
            for layer, w in ((1, w1), (2, w2)):
                whole = TILES[layer] - 1
                act.dma_start(stage[:, stage_at[layer]:stage_at[layer] + whole, :],
                              w[0:whole * P, :].rearrange("(t p) l -> p t l", p=P)).then_inc(w_in[layer], 16)
                for (ly, t), at in NATIVE.items():
                    if ly == layer:
                        k = min(P, F * H - t * P)
                        act.dma_start(wn[0:k, at, :], w[t * P:t * P + k, :]).then_inc(wn_in, 16)
            act.dma_start(ident[:], ident_in).then_inc(small_in, 16)

            act.wait_ge(x3_in, 48)
            act.activation(h[0][0:PAIR_ROWS, :], x3[0:PAIR_ROWS, :], ACT.Copy).then_inc(x3_ready, 1)
            act.wait_ge(w0_folded, 1)
            round_weights(0)
            for s in steps_of(-1):
                round_products(-1, s)
            act.wait_ge(w_in[1], 16)
            round_weights(1)
            copy_x3(-1, groups_over(-1, C_LAST))
            act.wait_ge(small_in, 64)
            act.wait_ge(sums_zero, 2)
            relu_out(0, -1, None, groups_over(-1, C_LAST), sum01[0:H, :])
            act.wait_ge(w_in[2], 16)
            round_weights(2)
            iteration(0, 0)
            with act.Fori(0, (D - 4) // 2) as pair:
                iteration(2 * pair + 1, 1)
                iteration(2 * pair + 2, 0)
            iteration(D - 3, 1)
            iteration(D - 2, 0)
            iteration(D - 1, 1)
            iteration(D, 0)
            relu_last(D)
            act.wait_ge(turned, 2)
            act.activation(z[:, 0, 0:2, :].rearrange("p a (k c) -> p (a k) c", c=2 * L)[:, :, L:2 * L],
                           acc[2][:].rearrange("p (k c) -> p k c", c=L), ACT.Copy).then_inc(out_ready, 1)

        @block.gpsimd
        def _(pool):
            def split_products(i, s):
                layer, g, _ = STEPS[s]
                _, p, _ = MIX[layer][g]
                rw, slot = rows(layer), slot_of(i, s)
                if p == 0:
                    return
                pool.wait_ge(zh_ready, rounded_over(i, s))
                pool.tensor_tensor(zl[0:rw, slot, 0:p, :], z[0:rw, slot, 0:p, :],
                                   zh[0:rw, zh_at(slot):zh_at(slot) + p, :].bitcast(F32),
                                   ALU.subtract).then_inc(pool_split, 1)

            def add_last(i):
                pool.wait_ge(acc_read[2], i)
                if not (isinstance(i, int) and i < 2):
                    pool.wait_ge(added2, i - 1)
                pool.tensor_tensor(sum2[:], sum2[:], direct2[:], ALU.add).then_inc(added2, 1)

            def add_first(i):
                number = isinstance(i, int)
                lo = 0
                pool.wait_ge(acc_read[1], i + 1)
                if number and i == D - 1:
                    lo = H
                    pool.wait_ge(pool_split, pool_over(D, STEP[2, TAIL]))
                else:
                    pool.wait_ge(acc_read[0], i + 2)
                if not (number and i < 1):
                    pool.wait_ge(added01, i)
                pool.tensor_tensor(sum01[lo:L, :], sum01[lo:L, :], direct01[lo:L, :], ALU.add).then_inc(added01, 1)

            def iteration(i, par):
                number = isinstance(i, int)
                for s in steps_of(i):
                    split_products(i, s)
                    if s == 3 and not (number and i < 1):
                        add_first(i - 1)
                    if s == B_LAST + LAG + 1 and not (number and i < 1):
                        add_last(i)

            for s in steps_of(-1):
                split_products(-1, s)
            pool.wait_ge(w_rounded, sum(SPLIT_GROUPS.values()))
            for g, (v, p, _) in enumerate(MIX[2]):
                if v + p:
                    at, s0 = SPLIT[2, GROUP * g], stage_at[2] + GROUP * g
                    pool.tensor_tensor(wl[:, at:at + v + p, :], stage[:, s0:s0 + v + p, :],
                                       wh[:, at:at + v + p, :].bitcast(F32), ALU.subtract).then_inc(w_split[2], 1)
            pool.wait_ge(acc_read[0], 1)
            iteration(0, 0)
            with pool.Fori(0, (D - 4) // 2) as pair:
                iteration(2 * pair + 1, 1)
                iteration(2 * pair + 2, 0)
            iteration(D - 3, 1)
            iteration(D - 2, 0)
            iteration(D - 1, 1)
            for s in steps_of(D):
                split_products(D, s)
                if s == STEP[2, TAIL]:
                    add_first(D - 1)
                    pool.wait_ge(added01, D)
            add_last(D)

        @block.tensor
        def _(pe):
            def group(i, s):
                layer, g, _ = STEPS[s]
                v, p, _ = MIX[layer][g]
                slot, n = slot_of(i, s), tiles_of(layer, g)
                number = isinstance(i, int)
                first, last = g == 0, GROUP * (g + 1) >= TILES[layer]
                if first:
                    before_it = i + 1 if layer == 0 else i
                    if not (number and before_it < 1):
                        pe.wait_ge(acc_read[layer], before_it)
                    if number and i == (-1 if layer == 0 else 0):
                        pe.wait_ge(w_split[layer], SPLIT_GROUPS[layer])
                        if layer == 0:
                            pe.wait_ge(w0_native, sum(ly == 0 for ly, _ in NATIVE))
                        if layer == 1:
                            pe.wait_ge(wn_in, 16 * sum(ly > 0 for ly, _ in NATIVE))

                def depth(t):
                    return min(PAIR_ROWS, F * SHIFTS - PAIR_ROWS * t) if layer == 0 else min(P, F * H - P * t)

                order = [*range(v + p, n), *range(v + p)]
                for k in order:
                    if k == v + p:
                        pe.wait_ge(z_made, groups_over(i, s))
                    elif k == 0 and v:
                        pe.wait_ge(vect_split, vect_over(i, s))
                    elif k == 0:
                        pe.wait_ge(pool_split, pool_over(i, s))
                    t = GROUP * g + k
                    d = depth(t)
                    if k >= v + p:
                        terms = [(wn[0:d, NATIVE[layer, t], :], z[0:d, slot, k, :])]
                    else:
                        at = SPLIT[layer, t]
                        hi, lo = zh[0:d, zh_at(slot) + k, :], zl[0:d, slot, k, :]
                        terms = [(wh[0:d, at, :], hi), (wl[0:d, at, :], hi), (wh[0:d, at, :], lo)]
                    for m, (w, zz) in enumerate(terms):
                        mm = pe.matmul(acc[layer][:], w, zz, start=first and k == order[0] and m == 0,
                                       stop=last and k == order[-1] and m == len(terms) - 1)
                mm.then_inc(group_used, 1)

            def iteration(i, par):
                for s in steps_of(i):
                    group(i, s)

            iteration(-1, 1)
            iteration(0, 0)
            with pe.Fori(0, (D - 4) // 2) as pair:
                iteration(2 * pair + 1, 1)
                iteration(2 * pair + 2, 0)
            iteration(D - 3, 1)
            iteration(D - 2, 0)
            iteration(D - 1, 1)
            iteration(D, 0)
            pe.wait_ge(small_in, 64)
            for layer, total, added, count in ((1, sum01, added01, D), (2, sum2, added2, D)):
                pe.wait_ge(added, count)
                pe.wait_ge(acc_read[layer], D)
                for k in range(B // P):
                    mm = pe.transpose(acc[layer][:, k * L:(k + 1) * L], total[:, k * P:(k + 1) * P], ident[:])
                mm.then_inc(turned, 1)


def kernel(**inputs):
    import numpy as np
    import concourse.bacc as bacc
    from concourse.bass_utils import run_bass_kernel_spmd

    xc = np.ascontiguousarray(inputs["r_x"]).transpose(2, 1, 0)
    xc = np.ascontiguousarray(np.concatenate([xc, xc], axis=1))
    w0 = np.ascontiguousarray(inputs["L0_rec_W0"])
    w0a = np.zeros((P, TILES[0], L), w0.dtype)
    w0b = np.zeros((P, TILES[0], L), w0.dtype)
    for s in range(SHIFTS):
        f = np.arange(F)
        g = (f + s) % F
        at = slice((s % 3) * F, (s % 3 + 1) * F)
        w0a[at, s // 3] = w0[f * F + g]
        if s:
            w0b[at, s // 3] = w0[g * F + f]
    arrays = {"x": xc, "w0a": w0a, "w0b": w0b, "w1": inputs["L0_rec_W1"], "w2": inputs["L0_rec_W2"],
              "b0": inputs["L0_rec_b0"], "b1": inputs["L0_rec_b1"], "b2": inputs["L0_rec_b2"],
              "ident": np.eye(P, dtype=np.float32)}
    arrays = {f"in_{k}": np.ascontiguousarray(v) for k, v in arrays.items()}
    nc = bacc.Bacc("TRN2", target_bir_lowering=False, num_devices=1)
    args = [nc.dram_tensor(k, v.shape, mybir.dt.from_np(v.dtype), kind="ExternalInput").ap()
            for k, v in arrays.items()]
    args.append(nc.dram_tensor("out", (B, 2 * L), F32, kind="ExternalOutput").ap())
    cin_kernel(nc, *args)
    return run_bass_kernel_spmd(nc, [arrays], core_ids=[0]).results[0]["out"]
```

```python
from contextlib import ExitStack

import concourse.bass as bass
from concourse import mybir

F32 = mybir.dt.float32
F32R = mybir.dt.float32r
ALU = mybir.AluOpType
ACT = mybir.ActivationFunctionType

P = 128
B = 512
D = 16
F = 39
L = 128
H = L // 2
GROUP = 2
XLOAD = 2
SHIFTS = F // 2 + 1
TILES = {0: 7, 1: 20, 2: 20}
RING = 8
LAG = {0: 5, 1: 6, 2: 6}
PAIR_ROWS = 3 * F

VV, PP, PN, N = (2, 0, 0), (0, 2, 0), (0, 1, 1), (0, 0, 1)
MIX = {0: [VV, PN, PP, N],
       1: [VV, PN, PP, PN, VV, PN, PP, PN, PP, PN],
       2: [PP, PN, VV, PN, PP, PN, VV, PN, PP, PN]}

TAIL = 6
STEPS = ([(1, g, 0) for g in range(10)] + [(2, g, -1) for g in range(TAIL, 10)]
         + [(0, g, 1) for g in range(4)] + [(2, g, 0) for g in range(TAIL)])
STEP = {(layer, g): s for s, (layer, g, _) in enumerate(STEPS)}
A_LAST, B_LAST, C_LAST = STEP[1, 9], STEP[2, 9], STEP[0, 3]
STEADY = 1
assert len(STEPS) % RING == 0


def steps_of(i):
    if not isinstance(i, int):
        return list(range(len(STEPS)))
    return [s for s, (_, _, off) in enumerate(STEPS) if 0 <= i + off < D]


def tally(counts):
    total, at = 0, {}
    for i in range(-1, D + 1):
        for s in steps_of(i):
            total += counts(*MIX[STEPS[s][0]][STEPS[s][1]])
            at[i, s] = total
    each = sum(counts(*MIX[layer][g]) for layer, g, _ in STEPS)

    def after(i, s):
        if isinstance(i, int):
            return at[i, s]
        return (i - STEADY) * each + at[STEADY, s]
    return after


groups_over = tally(lambda v, p, n: 1)
vect_over = tally(lambda v, p, n: int(v > 0))
pool_over = tally(lambda v, p, n: int(p > 0))
rounded_over = tally(lambda v, p, n: int(v + p > 0))


def slot_of(i, s):
    return (groups_over(i if isinstance(i, int) else STEADY, s) - 1) % RING


def zh_at(slot):
    return slot // 2 * 3 + slot % 2 * 2


def tiles_of(layer, g):
    return min(GROUP, TILES[layer] - GROUP * g)


SPLIT, NATIVE = {}, {}
for _layer in (0, 1, 2):
    for _t in range(TILES[_layer]):
        _v, _p, _n = MIX[_layer][_t // GROUP]
        assert _v + _p + _n == tiles_of(_layer, _t // GROUP) and _v + _p <= 2 - STEP[_layer, _t // GROUP] % 2
        _to = SPLIT if _t % GROUP < _v + _p else NATIVE
        _to[_layer, _t] = len(_to)


W2_STAGED = [6, 7, 8, 9, STEP[0, 0]]
W2_ROUNDED = [8, 9, STEP[0, 0], STEP[0, 1], STEP[0, 2]]
SPLIT_GROUPS = {layer: sum(v + p > 0 for v, p, _ in MIX[layer]) for layer in MIX}


def cin_kernel(nc, x, w0a, w0b, w1, w2, b, ident_dram, out):
    with ExitStack() as ctx:
        def sb(name, shape, dt):
            return ctx.enter_context(nc.sbuf_tensor(name, shape, dt))

        def pb(name, shape):
            return ctx.enter_context(nc.psum_tensor(name, shape, F32))

        def sem(name):
            return ctx.enter_context(nc.semaphore(name))

        xb = [sb(f"xb{k}", [P, TILES[1], B], F32) for k in range(2)]
        xr = sb("xr", [P, TILES[0], B], F32)
        x3 = sb("x3", [P, B], F32)
        with nc.sbuf_tensor("z", [P, RING, GROUP, B], F32) as z:
            pass
        zl = sb("zl", [P, RING, GROUP, B], F32R)
        zh = sb("zh", [P, RING // 2 * 3, B], F32R)
        wh = sb("wh", [P, len(SPLIT), L], F32R)
        wl = sb("wl", [P, len(SPLIT), L], F32R)
        wn = sb("wn", [P, len(NATIVE), L], F32)
        direct01 = sb("direct01", [P, B], F32)
        direct2 = sb("direct2", [P, B], F32)
        sum01 = sb("sum01", [P, B], F32)
        sum2 = sb("sum2", [P, B], F32)
        bias = sb("bias", [P, 3], F32)
        ident = sb("ident", [P, P], F32)

        acc = {n: pb(f"acc{n}", [P, B]) for n in (0, 1, 2)}
        h = {1: pb("h_in1", [P, B]), 2: pb("h_in2", [P, B]), 0: pb("x3p", [P, B])}
        zv = pb("zv", [P, 2, B])

        stage = xb[1][:].rearrange("p t (a l) -> p (t a) l", l=L)
        stage_at = {0: 2 * TILES[0], 1: 3 * TILES[0], 2: B // L * (2 * TAIL)}
        assert stage_at[1] + TILES[1] <= stage_at[2] <= B // L * TILES[1] - TILES[2]

        x_in = [[sem(f"x_in{k}_{g}") for g in range(5)] for k in range(2)]
        xr_in = [sem(f"xr_in{g}") for g in range(2)]
        x3_in = sem("x3_in")
        x3_ready = sem("x3_ready")
        w0_in, w_in = sem("w0_in"), {1: sem("w1_in"), 2: sem("w2_in")}
        bias_in, ident_in = sem("bias_in"), sem("ident_in")
        w0_folded, w0_native = sem("w0_folded"), sem("w0_native")
        w_rounded, w_split = sem("w_rounded"), {n: sem(f"w{n}_split") for n in (0, 1, 2)}
        z_made = sem("z_made")
        zh_ready = sem("zh_ready")
        vect_split, pool_split = sem("vect_split"), sem("pool_split")
        group_used = sem("group_used")
        h_ready = {1: sem("h1_ready"), 2: sem("h2_ready")}
        acc_read = {n: sem(f"acc{n}_read") for n in (0, 1, 2)}
        sums_zero = sem("sums_zero")
        added01, added2 = sem("added01"), sem("added2")
        turned, out_ready, out_done = sem("turned"), sem("out_ready"), sem("out_done")

        def rows(layer):
            return PAIR_ROWS if layer == 0 else P

        block = ctx.enter_context(nc.Block())

        @block.sync
        def _(sp):
            wide = XLOAD * GROUP
            x_loads = TILES[1] // wide

            def load_x(chunk, par, q):
                for half in range(2):
                    src = x[chunk, 2 * wide * q + half, :]
                    src = bass.AP(tensor=src.tensor, offset=src.offset, ap=[[0, H], [2 * B, wide], [1, B]])
                    sp.dma_start(xb[par][half * H:(half + 1) * H, wide * q:wide * (q + 1), :],
                                 src).then_inc(x_in[par][q], 16)

            def load_shifted(chunk, q):
                t0, n = wide * q, min(wide, TILES[0] - wide * q)
                for j in range(3):
                    src = x[chunk, 3 * t0 + j, :]
                    src = bass.AP(tensor=src.tensor, offset=src.offset, ap=[[B, F], [3 * B, n], [1, B]])
                    sp.dma_start(xr[j * F:(j + 1) * F, t0:t0 + n, :], src).then_inc(xr_in[q], 16)

            def load_x3(chunk):
                for j in range(3):
                    sp.dma_start(x3[j * F:(j + 1) * F, :], x[chunk, 0:F, :]).then_inc(x3_in, 16)

            def iteration(i, par):
                first, last = (i == 0, i == D - 2) if isinstance(i, int) else (False, False)
                if not last:
                    sp.wait_ge(x3_ready, i + 2)
                    load_x3(i + 2)
                for q in range(x_loads):
                    g = XLOAD * q + XLOAD - 1
                    if first:
                        split = 1 if g < TAIL else 2
                        sp.wait_ge(w_split[split], SPLIT_GROUPS[split])
                    elif g < TAIL:
                        sp.wait_ge(z_made, groups_over(i - 1, STEP[2, g]))
                    else:
                        sp.wait_ge(z_made, groups_over(i, STEP[2, g]))
                    load_x(i + 1, 1 - par, q)
                if not last:
                    for q in range(2):
                        sp.wait_ge(z_made, groups_over(i, STEP[0, XLOAD * q + 1]))
                        load_shifted(i + 2, q)

            def load_weights(layer, w):
                whole, (_, t0), n = TILES[layer] - 1, min(k for k in NATIVE if k[0] == layer), TILES[layer] // 4 - 1
                at = NATIVE[layer, t0]
                assert [t for ly, t in NATIVE if ly == layer] == [t0 + 4 * k for k in range(n + 1)]
                sp.dma_start(stage[:, stage_at[layer]:stage_at[layer] + whole, :],
                             w[0:whole * P, :].rearrange("(t p) l -> p t l", p=P)).then_inc(w_in[layer], 16)
                src = w[t0 * P:(t0 + 1) * P, :]
                src = bass.AP(tensor=src.tensor, offset=src.offset, ap=[[L, P], [4 * P * L, n], [1, L]])
                sp.dma_start(wn[:, at:at + n, :], src).then_inc(w_in[layer], 16)
                sp.dma_start(wn[0:F * H - whole * P, at + n, :], w[whole * P:F * H, :]).then_inc(w_in[layer], 16)

            load_x3(0)
            for q in range(2):
                load_shifted(0, q)
            load_weights(1, w1)
            sp.dma_start(bias[:], b).then_inc(bias_in, 16)
            for q in range(2):
                load_x(0, 0, q)
            sp.wait_ge(x3_ready, 1)
            load_x3(1)
            load_x(0, 0, 2)
            load_weights(2, w2)
            for q in range(3, x_loads):
                load_x(0, 0, q)
            for q in range(2):
                sp.wait_ge(z_made, groups_over(-1, STEP[0, XLOAD * q + 1]))
                load_shifted(1, q)
            sp.dma_start(ident[:], ident_dram).then_inc(ident_in, 16)
            iteration(0, 0)
            with sp.Fori(0, (D - 4) // 2) as pair:
                iteration(2 * pair + 1, 1)
                iteration(2 * pair + 2, 0)
            iteration(D - 3, 1)
            iteration(D - 2, 0)
            sp.wait_ge(out_ready, 2)
            sp.dma_start(out.rearrange("(k p) c -> p k c", p=P),
                         z[:, 0, 0:2, :].rearrange("p a (k c) -> p (a k) c", c=2 * L)).then_inc(out_done, 16)
            sp.wait_ge(out_done, 16)

        @block.vector
        def _(dve):
            def split_weights(layer, groups):
                for g in groups:
                    v, p, _ = MIX[layer][g]
                    if v + p:
                        at = SPLIT[layer, GROUP * g]
                        s0 = stage_at[layer] + GROUP * g
                        dve.tensor_tensor(wl[:, at:at + v + p, :], stage[:, s0:s0 + v + p, :],
                                          wh[:, at:at + v + p, :].bitcast(F32), ALU.subtract).then_inc(w_split[layer], 1)

            def make(i, s, par):
                layer, g, off = STEPS[s]
                v, _, _ = MIX[layer][g]
                rw, n, slot = rows(layer), tiles_of(layer, g), slot_of(i, s)
                over = groups_over(i, s)
                if layer == 0:
                    dve.wait_ge(xr_in[g // XLOAD], 48 * (i + 2))
                    if g == 0:
                        dve.wait_ge(x3_ready, i + 2)
                else:
                    nth = (i + off) // 2 if isinstance(i, int) else (i + off - (par + off) % 2) // 2
                    dve.wait_ge(x_in[(par + off) % 2][g // XLOAD], 32 * (nth + 1))
                    if g == 0:
                        dve.wait_ge(h_ready[layer], 2 * (i + 1))
                if v:
                    if not (isinstance(i, int) and vect_over(i, s) == 1):
                        dve.wait_ge(vect_split, vect_over(i, s) - 1)
                    to = zv[0:rw, 0:n, :]
                else:
                    if not (isinstance(i, int) and over <= RING):
                        dve.wait_ge(group_used, over - RING)
                    to = z[0:rw, slot, 0:n, :]
                t0 = GROUP * g
                xs = xr if layer == 0 else xb[(par + off) % 2]
                dve.tensor_tensor(to, xs[0:rw, t0:t0 + n, :], h[layer][0:rw, :].unsqueeze(1).to_broadcast([rw, n, B]),
                                  ALU.mult).then_inc(z_made, 1)

            def split(i, s):
                rw, slot = rows(STEPS[s][0]), slot_of(i, s)
                dve.wait_ge(zh_ready, rounded_over(i, s))
                dve.tensor_tensor(zl[0:rw, slot, :, :], zv[0:rw, :, :],
                                  zh[0:rw, zh_at(slot):zh_at(slot) + 2, :].bitcast(F32),
                                  ALU.subtract).then_inc(vect_split, 1)

            def iteration(i, par):
                waiting = None
                for s in steps_of(i):
                    if isinstance(i, int) and i == 0 and s in W2_ROUNDED:
                        two = W2_ROUNDED.index(s)
                        dve.wait_ge(w_rounded, SPLIT_GROUPS[0] + SPLIT_GROUPS[1] + 2 * two + 2)
                        split_weights(2, (2 * two, 2 * two + 1))
                    make(i, s, par)
                    if waiting is not None:
                        split(i, waiting)
                    layer, g, _ = STEPS[s]
                    waiting = s if MIX[layer][g][0] else None
                assert waiting is None

            dve.memset(sum01[:], 0.0).then_inc(sums_zero, 1)
            dve.memset(sum2[:], 0.0).then_inc(sums_zero, 1)
            dve.wait_ge(w0_in, 32)
            folded = stage_at[0]
            dve.tensor_tensor(stage[:, folded:folded + TILES[0], :], stage[:, 0:TILES[0], :],
                              stage[:, TILES[0]:2 * TILES[0], :], ALU.add).then_inc(w0_folded, 1)
            dve.wait_ge(w0_folded, 1)
            for (layer, t), at in NATIVE.items():
                if layer == 0:
                    dve.tensor_copy(wn[:, at, :], stage[:, folded + t, :]).then_inc(w0_native, 1)
            dve.wait_ge(w_rounded, SPLIT_GROUPS[0])
            split_weights(0, range(4))
            iteration(-1, 1)
            dve.wait_ge(w_rounded, SPLIT_GROUPS[0] + SPLIT_GROUPS[1])
            split_weights(1, range(10))
            iteration(0, 0)
            with dve.Fori(0, (D - 4) // 2) as pair:
                iteration(2 * pair + 1, 1)
                iteration(2 * pair + 2, 0)
            iteration(D - 3, 1)
            iteration(D - 2, 0)
            iteration(D - 1, 1)
            iteration(D, 0)
            dve.wait_ge(turned, 1)
            dve.tensor_copy(z[:, 0, 0:2, :].rearrange("p a (k c) -> p (a k) c", c=2 * L)[:, :, 0:L],
                            acc[1][:].rearrange("p (k c) -> p k c", c=L)).then_inc(out_ready, 1)

        @block.scalar
        def _(act):
            def round_weights(layer, groups):
                for g in groups:
                    v, p, _ = MIX[layer][g]
                    if v + p:
                        at = SPLIT[layer, GROUP * g]
                        s0 = stage_at[layer] + GROUP * g
                        act.activation(wh[:, at:at + v + p, :], stage[:, s0:s0 + v + p, :], ACT.Copy).then_inc(w_rounded, 1)

            def round_products(i, s):
                layer, g, _ = STEPS[s]
                v, p, _ = MIX[layer][g]
                rw, slot, k = rows(layer), slot_of(i, s), v + p
                if k == 0:
                    return
                if not (isinstance(i, int) and groups_over(i, s) <= RING):
                    act.wait_ge(group_used, groups_over(i, s) - RING)
                act.wait_ge(z_made, groups_over(i, s))
                src = zv[0:rw, 0:k, :] if v else z[0:rw, slot, 0:k, :]
                act.activation(zh[0:rw, zh_at(slot):zh_at(slot) + k, :], src, ACT.Copy).then_inc(zh_ready, 1)

            def relu_out(layer, i, h_free, group, direct):
                act.wait_ge(group_used, group)
                if layer == 1 and not (isinstance(i, int) and i < 1):
                    act.wait_ge(added01, i)
                if h_free is not None:
                    act.wait_ge(z_made, h_free)
                for half in range(2):
                    act.activation(h[layer + 1][half * H:(half + 1) * H, :], acc[layer][0:H, :], ACT.Relu,
                                   bias=bias[0:H, layer:layer + 1]).then_inc(h_ready[layer + 1], 1)
                act.activation(direct, acc[layer][H:L, :], ACT.Relu,
                               bias=bias[H:L, layer:layer + 1]).then_inc(acc_read[layer], 1)

            def relu_last(i):
                act.wait_ge(group_used, groups_over(i, B_LAST))
                if not (isinstance(i, int) and i < 2):
                    act.wait_ge(added2, i - 1)
                act.activation(direct2[:], acc[2][:], ACT.Relu, bias=bias[:, 2:3]).then_inc(acc_read[2], 1)

            def copy_x3(i, g_done):
                act.wait_ge(x3_in, 48 * (i + 3))
                if g_done is not None:
                    act.wait_ge(z_made, g_done)
                act.activation(h[0][0:PAIR_ROWS, :], x3[0:PAIR_ROWS, :], ACT.Copy).then_inc(x3_ready, 1)

            def iteration(i, par):
                number = isinstance(i, int)
                for s in steps_of(i):
                    if number and i == 0 and s in W2_STAGED:
                        act.wait_ge(w_in[2], 48)
                        two = W2_STAGED.index(s)
                        round_weights(2, (2 * two, 2 * two + 1))
                    if s == A_LAST + LAG[1] or (number and i == D - 1 and s == STEP[2, 0]):
                        relu_out(1, i, None if number and i < 1 else groups_over(i, B_LAST),
                                 groups_over(i, A_LAST), direct01[H:L, :])
                    if s == B_LAST + LAG[2] and not (number and i < 1):
                        relu_last(i)
                    if s == C_LAST + LAG[0] and not (number and i > D - 2):
                        relu_out(0, i, groups_over(i, A_LAST), groups_over(i, C_LAST), direct01[0:H, :])
                    round_products(i, s)
                    if s == C_LAST and not (number and i >= D - 2):
                        copy_x3(i, groups_over(i, C_LAST))

            act.dma_start(stage[:, 0:TILES[0], :], w0a).then_inc(w0_in, 16)
            act.dma_start(stage[:, TILES[0]:2 * TILES[0], :], w0b).then_inc(w0_in, 16)
            act.wait_ge(x3_in, 48)
            act.activation(h[0][0:PAIR_ROWS, :], x3[0:PAIR_ROWS, :], ACT.Copy).then_inc(x3_ready, 1)
            act.wait_ge(w0_folded, 1)
            round_weights(0, range(4))
            for s in steps_of(-1):
                round_products(-1, s)
            act.wait_ge(w_in[1], 48)
            round_weights(1, range(10))
            act.wait_ge(bias_in, 16)
            act.wait_ge(sums_zero, 2)
            relu_out(0, -1, None, groups_over(-1, C_LAST), sum01[0:H, :])
            copy_x3(-1, groups_over(-1, C_LAST))
            iteration(0, 0)
            with act.Fori(0, (D - 4) // 2) as pair:
                iteration(2 * pair + 1, 1)
                iteration(2 * pair + 2, 0)
            iteration(D - 3, 1)
            iteration(D - 2, 0)
            iteration(D - 1, 1)
            iteration(D, 0)
            relu_last(D)
            act.wait_ge(turned, 2)
            act.activation(z[:, 0, 0:2, :].rearrange("p a (k c) -> p (a k) c", c=2 * L)[:, :, L:2 * L],
                           acc[2][:].rearrange("p (k c) -> p k c", c=L), ACT.Copy).then_inc(out_ready, 1)

        @block.gpsimd
        def _(pool):
            def split_products(i, s):
                layer, g, _ = STEPS[s]
                _, p, _ = MIX[layer][g]
                rw, slot = rows(layer), slot_of(i, s)
                if p == 0:
                    return
                pool.wait_ge(zh_ready, rounded_over(i, s))
                pool.tensor_tensor(zl[0:rw, slot, 0:p, :], z[0:rw, slot, 0:p, :],
                                   zh[0:rw, zh_at(slot):zh_at(slot) + p, :].bitcast(F32),
                                   ALU.subtract).then_inc(pool_split, 1)

            def add_last(i):
                pool.wait_ge(acc_read[2], i)
                if not (isinstance(i, int) and i < 2):
                    pool.wait_ge(added2, i - 1)
                pool.tensor_tensor(sum2[:], sum2[:], direct2[:], ALU.add).then_inc(added2, 1)

            def add_first(i):
                number = isinstance(i, int)
                lo = 0
                pool.wait_ge(acc_read[1], i + 1)
                if number and i == D - 1:
                    lo = H
                    pool.wait_ge(pool_split, pool_over(D, STEP[2, TAIL]))
                else:
                    pool.wait_ge(acc_read[0], i + 2)
                if not (number and i < 1):
                    pool.wait_ge(added01, i)
                pool.tensor_tensor(sum01[lo:L, :], sum01[lo:L, :], direct01[lo:L, :], ALU.add).then_inc(added01, 1)

            def iteration(i, par):
                number = isinstance(i, int)
                for s in steps_of(i):
                    split_products(i, s)
                    if s == 3 and not (number and i < 1):
                        add_first(i - 1)
                    if s == B_LAST + LAG[2] + 1 and not (number and i < 1):
                        add_last(i)

            for s in steps_of(-1):
                split_products(-1, s)
            pool.wait_ge(acc_read[0], 1)
            iteration(0, 0)
            with pool.Fori(0, (D - 4) // 2) as pair:
                iteration(2 * pair + 1, 1)
                iteration(2 * pair + 2, 0)
            iteration(D - 3, 1)
            iteration(D - 2, 0)
            iteration(D - 1, 1)
            for s in steps_of(D):
                split_products(D, s)
                if s == STEP[2, TAIL]:
                    add_first(D - 1)
                    pool.wait_ge(added01, D)
            add_last(D)

        @block.tensor
        def _(pe):
            def group(i, s):
                layer, g, _ = STEPS[s]
                v, p, _ = MIX[layer][g]
                slot, n = slot_of(i, s), tiles_of(layer, g)
                number = isinstance(i, int)
                first, last = g == 0, GROUP * (g + 1) >= TILES[layer]
                if first:
                    before_it = i + 1 if layer == 0 else i
                    if not (number and before_it < 1):
                        pe.wait_ge(acc_read[layer], before_it)
                    if number and i == (-1 if layer == 0 else 0):
                        pe.wait_ge(w_split[layer], SPLIT_GROUPS[layer])
                        if layer == 0:
                            pe.wait_ge(w0_native, sum(ly == 0 for ly, _ in NATIVE))
                        else:
                            pe.wait_ge(w_in[layer], 48)

                def depth(t):
                    return min(PAIR_ROWS, F * SHIFTS - PAIR_ROWS * t) if layer == 0 else min(P, F * H - P * t)

                order = [*range(v + p, n), *range(v + p)]
                for k in order:
                    if k == v + p:
                        pe.wait_ge(z_made, groups_over(i, s))
                    elif k == 0 and v:
                        pe.wait_ge(vect_split, vect_over(i, s))
                    elif k == 0:
                        pe.wait_ge(pool_split, pool_over(i, s))
                    t = GROUP * g + k
                    d = depth(t)
                    if k >= v + p:
                        terms = [(wn[0:d, NATIVE[layer, t], :], z[0:d, slot, k, :])]
                    else:
                        at = SPLIT[layer, t]
                        hi, lo = zh[0:d, zh_at(slot) + k, :], zl[0:d, slot, k, :]
                        terms = [(wh[0:d, at, :], hi), (wl[0:d, at, :], hi), (wh[0:d, at, :], lo)]
                    for m, (w, zz) in enumerate(terms):
                        mm = pe.matmul(acc[layer][:], w, zz, start=first and k == order[0] and m == 0,
                                       stop=last and k == order[-1] and m == len(terms) - 1)
                mm.then_inc(group_used, 1)

            def iteration(i, par):
                for s in steps_of(i):
                    group(i, s)

            iteration(-1, 1)
            iteration(0, 0)
            with pe.Fori(0, (D - 4) // 2) as pair:
                iteration(2 * pair + 1, 1)
                iteration(2 * pair + 2, 0)
            iteration(D - 3, 1)
            iteration(D - 2, 0)
            iteration(D - 1, 1)
            iteration(D, 0)
            pe.wait_ge(ident_in, 16)
            for layer, total, added, count in ((1, sum01, added01, D), (2, sum2, added2, D)):
                pe.wait_ge(added, count)
                pe.wait_ge(acc_read[layer], D)
                for k in range(B // P):
                    mm = pe.transpose(acc[layer][:, k * L:(k + 1) * L], total[:, k * P:(k + 1) * P], ident[:])
                mm.then_inc(turned, 1)


def kernel(**inputs):
    import numpy as np
    import concourse.bacc as bacc
    from concourse.bass_utils import run_bass_kernel_spmd

    xc = np.ascontiguousarray(inputs["r_x"]).transpose(2, 1, 0)
    xc = np.ascontiguousarray(np.concatenate([xc, xc], axis=1))
    w0 = np.ascontiguousarray(inputs["L0_rec_W0"])
    w0a = np.zeros((P, TILES[0], L), w0.dtype)
    w0b = np.zeros((P, TILES[0], L), w0.dtype)
    for s in range(SHIFTS):
        f = np.arange(F)
        g = (f + s) % F
        at = slice((s % 3) * F, (s % 3 + 1) * F)
        w0a[at, s // 3] = w0[f * F + g]
        if s:
            w0b[at, s // 3] = w0[g * F + f]
    arrays = {"x": xc, "w0a": w0a, "w0b": w0b, "w1": inputs["L0_rec_W1"], "w2": inputs["L0_rec_W2"],
              "b": np.stack([inputs[f"L0_rec_b{n}"] for n in range(3)], axis=1),
              "ident": np.eye(P, dtype=np.float32)}
    arrays = {f"in_{k}": np.ascontiguousarray(v) for k, v in arrays.items()}
    nc = bacc.Bacc("TRN2", target_bir_lowering=False, num_devices=1)
    args = [nc.dram_tensor(k, v.shape, mybir.dt.from_np(v.dtype), kind="ExternalInput").ap()
            for k, v in arrays.items()]
    args.append(nc.dram_tensor("out", (B, 2 * L), F32, kind="ExternalOutput").ap())
    cin_kernel(nc, *args)
    return run_bass_kernel_spmd(nc, [arrays], core_ids=[0]).results[0]["out"]
```

```python
from contextlib import ExitStack

import concourse.bass as bass
from concourse import mybir

F32 = mybir.dt.float32
F32R = mybir.dt.float32r
ALU = mybir.AluOpType
ACT = mybir.ActivationFunctionType

P = 128
B = 512
D = 16
F = 39
L = 128
H = L // 2
GROUP = 2
XLOAD = 2
SHIFTS = F // 2 + 1
TILES = {0: 7, 1: 20, 2: 20}
RING = 8
LAG = {0: 5, 1: 7, 2: 7}
PAIR_ROWS = 3 * F

VV, PP, PN, N = (2, 0, 0), (0, 2, 0), (0, 1, 1), (0, 0, 1)
PS = PP
MIX = {0: [VV, PN, PP, N],
       1: [VV, PN, PP, PN, VV, PN, PP, PN, PN, PS],
       2: [PP, PN, VV, PN, PP, PN, VV, PN, PN, PS]}
HALF = F // 2

TAIL = 6
ORDER = [*range(8), 9, 8]
STEPS = ([(1, g, 0) for g in ORDER] + [(2, g, -1) for g in ORDER[TAIL:]]
         + [(0, g, 1) for g in range(4)] + [(2, g, 0) for g in ORDER[:TAIL]])
STEP = {(layer, g): s for s, (layer, g, _) in enumerate(STEPS)}
A_LAST, B_LAST, C_LAST = STEP[1, ORDER[-1]], STEP[2, ORDER[-1]], STEP[0, 3]
STEADY = 1
assert len(STEPS) % RING == 0


def steps_of(i):
    if not isinstance(i, int):
        return list(range(len(STEPS)))
    return [s for s, (_, _, off) in enumerate(STEPS) if 0 <= i + off < D]


def tally(counts):
    total, at = 0, {}
    for i in range(-1, D + 1):
        for s in steps_of(i):
            total += counts(*MIX[STEPS[s][0]][STEPS[s][1]])
            at[i, s] = total
    each = sum(counts(*MIX[layer][g]) for layer, g, _ in STEPS)

    def after(i, s):
        if isinstance(i, int):
            return at[i, s]
        return (i - STEADY) * each + at[STEADY, s]
    return after


groups_over = tally(lambda v, p, n: 1)
vect_over = tally(lambda v, p, n: int(v > 0))
pool_over = tally(lambda v, p, n: int(p > 0))
rounded_over = tally(lambda v, p, n: int(v + p > 0))


def slot_of(i, s):
    return (groups_over(i if isinstance(i, int) else STEADY, s) - 1) % RING


def zh_at(slot):
    return slot // 2 * 3 + slot % 2 * 2


def tiles_of(layer, g):
    return min(GROUP, TILES[layer] - GROUP * g)


SPLIT, NATIVE = {}, {}
for _layer in (0, 1, 2):
    for _t in range(TILES[_layer]):
        _v, _p, _n = MIX[_layer][_t // GROUP]
        assert _v + _p + _n == tiles_of(_layer, _t // GROUP)
        assert _v + _p - (_layer > 0 and _t // GROUP == HALF // GROUP) <= 2 - STEP[_layer, _t // GROUP] % 2
        _to = SPLIT if _t % GROUP < _v + _p else NATIVE
        _to[_layer, _t] = len(_to)


W2_STAGED = [6, 7, 8, 9, STEP[0, 0]]
W2_ROUNDED = [8, 9, STEP[0, 0], STEP[0, 1], STEP[0, 2]]
ODD_NATIVE = {layer: [t for ly, t in NATIVE if ly == layer and t % 4 != 3] for layer in MIX}
W_LOADS = {layer: 4 + len(ODD_NATIVE[layer]) for layer in MIX}
SPLIT_GROUPS = {layer: sum(v + p > 0 for v, p, _ in MIX[layer]) for layer in MIX}


def cin_kernel(nc, x, x_halves, w0a, w0b, w1, w2, b, ident_dram, out):
    with ExitStack() as ctx:
        def sb(name, shape, dt):
            return ctx.enter_context(nc.sbuf_tensor(name, shape, dt))

        def pb(name, shape):
            return ctx.enter_context(nc.psum_tensor(name, shape, F32))

        def sem(name):
            return ctx.enter_context(nc.semaphore(name))

        xb = [sb(f"xb{k}", [P, TILES[1], B], F32) for k in range(2)]
        xr = sb("xr", [P, TILES[0], B], F32)
        x3 = sb("x3", [P, B], F32)
        with nc.sbuf_tensor("z", [P, RING, GROUP, B], F32) as z:
            pass
        zl = sb("zl", [P, RING, GROUP, B], F32R)
        zh = sb("zh", [P, RING // 2 * 3, B], F32R)
        zh_half = {n: sb(f"zh_half{n}", [P, B], F32R) for n in (1, 2)}
        wh = sb("wh", [P, len(SPLIT), L], F32R)
        wl = sb("wl", [P, len(SPLIT), L], F32R)
        wn = sb("wn", [P, len(NATIVE), L], F32)
        direct01 = sb("direct01", [P, B], F32)
        direct2 = sb("direct2", [P, B], F32)
        sum01 = sb("sum01", [P, B], F32)
        sum2 = sb("sum2", [P, B], F32)
        bias = sb("bias", [P, 3], F32)
        ident = sb("ident", [P, P], F32)

        acc = {n: pb(f"acc{n}", [P, B]) for n in (0, 1, 2)}
        h = {1: pb("h_in1", [P, B]), 2: pb("h_in2", [P, B]), 0: pb("x3p", [P, B])}
        zv = pb("zv", [P, 2, B])

        stage = xb[1][:].rearrange("p t (a l) -> p (t a) l", l=L)
        stage_at = {0: 2 * TILES[0], 1: 3 * TILES[0], 2: B // L * (2 * TAIL)}
        assert stage_at[1] + TILES[1] <= stage_at[2] <= B // L * TILES[1] - TILES[2]

        x_in = [[sem(f"x_in{k}_{g}") for g in range(5)] for k in range(2)]
        xr_in = [sem(f"xr_in{g}") for g in range(2)]
        x3_in = sem("x3_in")
        x3_ready = sem("x3_ready")
        w0_in, w_in = sem("w0_in"), {1: sem("w1_in"), 2: sem("w2_in")}
        bias_in, ident_in = sem("bias_in"), sem("ident_in")
        w0_folded, w0_native = sem("w0_folded"), sem("w0_native")
        w_rounded, w_split = sem("w_rounded"), {n: sem(f"w{n}_split") for n in (0, 1, 2)}
        z_made = sem("z_made")
        zh_ready = sem("zh_ready")
        vect_split, pool_split = sem("vect_split"), sem("pool_split")
        group_used = sem("group_used")
        h_ready = {1: sem("h1_ready"), 2: sem("h2_ready")}
        acc_read = {n: sem(f"acc{n}_read") for n in (0, 1, 2)}
        before_half = {n: sem(f"before_half{n}") for n in (1, 2)}
        added01, added2 = sem("added01"), sem("added2")
        turned, out_ready, out_done = sem("turned"), sem("out_ready"), sem("out_done")

        def rows(layer):
            return PAIR_ROWS if layer == 0 else P

        block = ctx.enter_context(nc.Block())

        @block.sync
        def _(sp):
            wide = XLOAD * GROUP
            x_loads = TILES[1] // wide

            def load_x(chunk, par, q):
                for half in range(2):
                    src = x_halves[chunk, half, wide * q, :]
                    src = bass.AP(tensor=src.tensor, offset=src.offset, ap=[[0, H], [1, wide * B]])
                    sp.dma_start(xb[par][half * H:(half + 1) * H, wide * q:wide * (q + 1), :].rearrange("p t n -> p (t n)"),
                                 src).then_inc(x_in[par][q], 16)

            def load_shifted(chunk, q):
                t0, n = wide * q, min(wide, TILES[0] - wide * q)
                for j in range(3):
                    src = x[chunk, 3 * t0 + j, :]
                    src = bass.AP(tensor=src.tensor, offset=src.offset, ap=[[B, F], [3 * B, n], [1, B]])
                    sp.dma_start(xr[j * F:(j + 1) * F, t0:t0 + n, :], src).then_inc(xr_in[q], 16)

            def load_x3(chunk):
                for j in range(3):
                    sp.dma_start(x3[j * F:(j + 1) * F, :], x[chunk, 0:F, :]).then_inc(x3_in, 16)

            def iteration(i, par):
                first, last = (i == 0, i == D - 2) if isinstance(i, int) else (False, False)
                if not last:
                    sp.wait_ge(x3_ready, i + 2)
                    load_x3(i + 2)
                for q in range(x_loads):
                    g = max(XLOAD * q, XLOAD * q + 1, key=ORDER.index)
                    if first:
                        split = 1 if g < TAIL else 2
                        sp.wait_ge(w_split[split], SPLIT_GROUPS[split])
                    elif g < TAIL:
                        sp.wait_ge(z_made, groups_over(i - 1, STEP[2, g]))
                    else:
                        sp.wait_ge(z_made, groups_over(i, STEP[2, g]))
                    load_x(i + 1, 1 - par, q)
                if not last:
                    for q in range(2):
                        sp.wait_ge(z_made, groups_over(i, STEP[0, XLOAD * q + 1]))
                        load_shifted(i + 2, q)

            def load_weights(layer, w):
                whole = TILES[layer] - 1
                sp.dma_start(stage[:, stage_at[layer]:stage_at[layer] + whole, :],
                             w[0:whole * P, :].rearrange("(t p) l -> p t l", p=P)).then_inc(w_in[layer], 16)
                for half in range(2):
                    sp.dma_start(stage[half * H:(half + 1) * H, stage_at[layer] + HALF, :],
                                 w[whole * P:F * H, :]).then_inc(w_in[layer], 16)
                at, n = NATIVE[layer, 3], whole // 4
                assert [NATIVE[layer, 4 * k + 3] for k in range(n)] == list(range(at, at + n))
                src = w[3 * P:4 * P, :]
                src = bass.AP(tensor=src.tensor, offset=src.offset, ap=[[L, P], [4 * P * L, n], [1, L]])
                sp.dma_start(wn[:, at:at + n, :], src).then_inc(w_in[layer], 16)
                for t in ODD_NATIVE[layer]:
                    sp.dma_start(wn[:, NATIVE[layer, t], :], w[t * P:(t + 1) * P, :]).then_inc(w_in[layer], 16)

            load_x3(0)
            for q in range(2):
                load_shifted(0, q)
            load_weights(1, w1)
            sp.dma_start(bias[:], b).then_inc(bias_in, 16)
            for q in range(2):
                load_x(0, 0, q)
            sp.wait_ge(x3_ready, 1)
            load_x3(1)
            load_x(0, 0, 2)
            load_weights(2, w2)
            for q in range(3, x_loads):
                load_x(0, 0, q)
            for q in range(2):
                sp.wait_ge(z_made, groups_over(-1, STEP[0, XLOAD * q + 1]))
                load_shifted(1, q)
            sp.dma_start(ident[:], ident_dram).then_inc(ident_in, 16)
            iteration(0, 0)
            with sp.Fori(0, (D - 4) // 2) as pair:
                iteration(2 * pair + 1, 1)
                iteration(2 * pair + 2, 0)
            iteration(D - 3, 1)
            iteration(D - 2, 0)
            sp.wait_ge(out_ready, 2)
            sp.dma_start(out.rearrange("(k p) c -> p k c", p=P),
                         z[:, 0, 0:2, :].rearrange("p a (k c) -> p (a k) c", c=2 * L)).then_inc(out_done, 16)
            sp.wait_ge(out_done, 16)

        @block.vector
        def _(dve):
            def split_weights(layer, groups):
                for g in groups:
                    v, p, _ = MIX[layer][g]
                    if v + p:
                        at = SPLIT[layer, GROUP * g]
                        s0 = stage_at[layer] + GROUP * g
                        dve.tensor_tensor(wl[:, at:at + v + p, :], stage[:, s0:s0 + v + p, :],
                                          wh[:, at:at + v + p, :].bitcast(F32), ALU.subtract).then_inc(w_split[layer], 1)

            def make(i, s, par):
                layer, g, off = STEPS[s]
                v, _, _ = MIX[layer][g]
                rw, n, slot = rows(layer), tiles_of(layer, g), slot_of(i, s)
                over = groups_over(i, s)
                if layer == 0:
                    dve.wait_ge(xr_in[g // XLOAD], 48 * (i + 2))
                    if g == 0:
                        dve.wait_ge(x3_ready, i + 2)
                else:
                    nth = (i + off) // 2 if isinstance(i, int) else (i + off - (par + off) % 2) // 2
                    dve.wait_ge(x_in[(par + off) % 2][g // XLOAD], 32 * (nth + 1))
                    if g == 0:
                        dve.wait_ge(h_ready[layer], 2 * (i + 1))
                if v:
                    if not (isinstance(i, int) and vect_over(i, s) == 1):
                        dve.wait_ge(vect_split, vect_over(i, s) - 1)
                    to = zv[0:rw, 0:n, :]
                else:
                    if not (isinstance(i, int) and over <= RING):
                        dve.wait_ge(group_used, over - RING)
                    to = z[0:rw, slot, 0:n, :]
                t0 = GROUP * g
                xs = xr if layer == 0 else xb[(par + off) % 2]
                dve.tensor_tensor(to, xs[0:rw, t0:t0 + n, :], h[layer][0:rw, :].unsqueeze(1).to_broadcast([rw, n, B]),
                                  ALU.mult).then_inc(z_made, 1)

            def split(i, s):
                rw, slot = rows(STEPS[s][0]), slot_of(i, s)
                dve.wait_ge(zh_ready, rounded_over(i, s))
                dve.tensor_tensor(zl[0:rw, slot, :, :], zv[0:rw, :, :],
                                  zh[0:rw, zh_at(slot):zh_at(slot) + 2, :].bitcast(F32),
                                  ALU.subtract).then_inc(vect_split, 1)

            def iteration(i, par):
                waiting = None
                for s in steps_of(i):
                    if isinstance(i, int) and i == 0 and s in W2_ROUNDED:
                        two = W2_ROUNDED.index(s)
                        dve.wait_ge(w_rounded, SPLIT_GROUPS[0] + SPLIT_GROUPS[1] + 2 * two + 2)
                        split_weights(2, (2 * two, 2 * two + 1))
                    make(i, s, par)
                    if waiting is not None:
                        split(i, waiting)
                    layer, g, _ = STEPS[s]
                    waiting = s if MIX[layer][g][0] else None
                assert waiting is None

            dve.memset(sum01[:], 0.0).then_inc(added01, 1)
            dve.memset(sum2[:], 0.0).then_inc(added2, 1)
            dve.wait_ge(w0_in, 32)
            folded = stage_at[0]
            dve.tensor_tensor(stage[:, folded:folded + TILES[0], :], stage[:, 0:TILES[0], :],
                              stage[:, TILES[0]:2 * TILES[0], :], ALU.add).then_inc(w0_folded, 1)
            dve.wait_ge(w0_folded, 1)
            for (layer, t), at in NATIVE.items():
                if layer == 0:
                    dve.tensor_copy(wn[:, at, :], stage[:, folded + t, :]).then_inc(w0_native, 1)
            dve.wait_ge(w_rounded, SPLIT_GROUPS[0])
            split_weights(0, range(4))
            iteration(-1, 1)
            dve.wait_ge(w_rounded, SPLIT_GROUPS[0] + SPLIT_GROUPS[1])
            split_weights(1, range(10))
            iteration(0, 0)
            with dve.Fori(0, (D - 4) // 2) as pair:
                iteration(2 * pair + 1, 1)
                iteration(2 * pair + 2, 0)
            iteration(D - 3, 1)
            iteration(D - 2, 0)
            iteration(D - 1, 1)
            iteration(D, 0)
            dve.wait_ge(acc_read[2], D)
            dve.wait_ge(added2, D)
            dve.tensor_tensor(sum2[:], sum2[:], direct2[:], ALU.add).then_inc(added2, 1)
            dve.wait_ge(turned, 1)
            dve.tensor_copy(z[:, 0, 0:2, :].rearrange("p a (k c) -> p (a k) c", c=2 * L)[:, :, 0:L],
                            acc[1][:].rearrange("p (k c) -> p k c", c=L)).then_inc(out_ready, 1)

        @block.scalar
        def _(act):
            def round_weights(layer, groups):
                for g in groups:
                    v, p, _ = MIX[layer][g]
                    if v + p:
                        at = SPLIT[layer, GROUP * g]
                        s0 = stage_at[layer] + GROUP * g
                        act.activation(wh[:, at:at + v + p, :], stage[:, s0:s0 + v + p, :], ACT.Copy).then_inc(w_rounded, 1)

            def round_products(i, s):
                layer, g, _ = STEPS[s]
                v, p, _ = MIX[layer][g]
                rw, slot, k = rows(layer), slot_of(i, s), v + p
                if k == 0:
                    return
                if not (isinstance(i, int) and groups_over(i, s) <= RING):
                    act.wait_ge(group_used, groups_over(i, s) - RING)
                act.wait_ge(z_made, groups_over(i, s))
                if layer and g == HALF // GROUP:
                    act.activation(zh[:, zh_at(slot), :], z[:, slot, 0, :], ACT.Copy)
                    act.activation(zh_half[layer][H:P, :], z[H:P, slot, 1, :], ACT.Copy)
                    act.activation(zl[0:H, slot, 1, :], z[0:H, slot, 1, :], ACT.Copy).then_inc(zh_ready, 1)
                    return
                src = zv[0:rw, 0:k, :] if v else z[0:rw, slot, 0:k, :]
                act.activation(zh[0:rw, zh_at(slot):zh_at(slot) + k, :], src, ACT.Copy).then_inc(zh_ready, 1)

            def relu_out(layer, i, h_free, group, direct):
                act.wait_ge(group_used, group)
                if layer == 1:
                    act.wait_ge(added01, i + 1)
                if h_free is not None:
                    act.wait_ge(z_made, h_free)
                for half in range(2):
                    act.activation(h[layer + 1][half * H:(half + 1) * H, :], acc[layer][0:H, :], ACT.Relu,
                                   bias=bias[0:H, layer:layer + 1]).then_inc(h_ready[layer + 1], 1)
                act.activation(direct, acc[layer][H:L, :], ACT.Relu,
                               bias=bias[H:L, layer:layer + 1]).then_inc(acc_read[layer], 1)

            def relu_last(i):
                act.wait_ge(group_used, groups_over(i, B_LAST))
                act.wait_ge(added2, i)
                act.activation(direct2[:], acc[2][:], ACT.Relu, bias=bias[:, 2:3]).then_inc(acc_read[2], 1)

            def copy_x3(i, g_done):
                act.wait_ge(x3_in, 48 * (i + 3))
                if g_done is not None:
                    act.wait_ge(z_made, g_done)
                act.activation(h[0][0:PAIR_ROWS, :], x3[0:PAIR_ROWS, :], ACT.Copy).then_inc(x3_ready, 1)

            def iteration(i):
                number = isinstance(i, int)
                for s in steps_of(i):
                    if number and i == 0 and s in W2_STAGED:
                        act.wait_ge(w_in[2], 16 * W_LOADS[2])
                        two = W2_STAGED.index(s)
                        round_weights(2, (2 * two, 2 * two + 1))
                    if s == A_LAST + LAG[1] or (number and i == D - 1 and s == STEP[2, 0]):
                        relu_out(1, i, None if number and i < 1 else groups_over(i, B_LAST),
                                 groups_over(i, A_LAST), direct01[H:L, :])
                    if s == B_LAST + LAG[2] and not (number and i < 1):
                        relu_last(i)
                    if s == C_LAST + LAG[0] and not (number and i > D - 2):
                        relu_out(0, i, groups_over(i, A_LAST), groups_over(i, C_LAST), direct01[0:H, :])
                    round_products(i, s)
                    if s == C_LAST and not (number and i >= D - 2):
                        copy_x3(i, groups_over(i, C_LAST))

            act.dma_start(stage[:, 0:TILES[0], :], w0a).then_inc(w0_in, 16)
            act.dma_start(stage[:, TILES[0]:2 * TILES[0], :], w0b).then_inc(w0_in, 16)
            act.wait_ge(x3_in, 48)
            act.activation(h[0][0:PAIR_ROWS, :], x3[0:PAIR_ROWS, :], ACT.Copy).then_inc(x3_ready, 1)
            act.wait_ge(w0_folded, 1)
            round_weights(0, range(4))
            for s in steps_of(-1):
                round_products(-1, s)
            act.wait_ge(w_in[1], 16 * W_LOADS[1])
            round_weights(1, range(10))
            act.wait_ge(bias_in, 16)
            act.wait_ge(added01, 1)
            relu_out(0, -1, None, groups_over(-1, C_LAST), sum01[0:H, :])
            copy_x3(-1, groups_over(-1, C_LAST))
            iteration(0)
            with act.Fori(0, (D - 4) // 2) as pair:
                iteration(2 * pair + 1)
                iteration(2 * pair + 2)
            iteration(D - 3)
            iteration(D - 2)
            iteration(D - 1)
            iteration(D)
            relu_last(D)
            act.wait_ge(turned, 2)
            act.activation(z[:, 0, 0:2, :].rearrange("p a (k c) -> p (a k) c", c=2 * L)[:, :, L:2 * L],
                           acc[2][:].rearrange("p (k c) -> p k c", c=L), ACT.Copy).then_inc(out_ready, 1)

        @block.gpsimd
        def _(pool):
            def split_products(i, s):
                layer, g, _ = STEPS[s]
                _, p, _ = MIX[layer][g]
                rw, slot = rows(layer), slot_of(i, s)
                if p == 0:
                    return
                pool.wait_ge(zh_ready, rounded_over(i, s))
                if layer and g == HALF // GROUP:
                    pool.tensor_tensor(zl[:, slot, 0, :], z[:, slot, 0, :], zh[:, zh_at(slot), :].bitcast(F32),
                                       ALU.subtract).then_inc(before_half[layer], 1)
                    pool.wait_ge(before_half[layer], i + 2 - layer)
                    pool.tensor_tensor(zl[H:P, slot, 1, :], z[H:P, slot, 1, :], zh_half[layer][H:P, :].bitcast(F32),
                                       ALU.subtract).then_inc(pool_split, 1)
                    pool.wait_ge(pool_split, pool_over(i, s))
                    return
                hi = zh[0:rw, zh_at(slot):zh_at(slot) + p, :]
                pool.tensor_tensor(zl[0:rw, slot, 0:p, :], z[0:rw, slot, 0:p, :], hi.bitcast(F32),
                                   ALU.subtract).then_inc(pool_split, 1)

            def add_last(i):
                pool.wait_ge(acc_read[2], i)
                pool.wait_ge(added2, i)
                pool.tensor_tensor(sum2[:], sum2[:], direct2[:], ALU.add).then_inc(added2, 1)

            def add_first(i):
                number = isinstance(i, int)
                lo = 0
                pool.wait_ge(acc_read[1], i + 1)
                if number and i == D - 1:
                    lo = H
                    pool.wait_ge(pool_split, pool_over(D, STEP[2, TAIL]))
                else:
                    pool.wait_ge(acc_read[0], i + 2)
                pool.wait_ge(added01, i + 1)
                pool.tensor_tensor(sum01[lo:L, :], sum01[lo:L, :], direct01[lo:L, :], ALU.add).then_inc(added01, 1)

            def iteration(i):
                number = isinstance(i, int)
                for s in steps_of(i):
                    split_products(i, s)
                    if s == 1 and not (number and i < 1):
                        add_first(i - 1)
                    if s == B_LAST + LAG[2] + 1 and not (number and i < 1):
                        add_last(i)

            for s in steps_of(-1):
                split_products(-1, s)
            pool.wait_ge(acc_read[0], 1)
            iteration(0)
            with pool.Fori(0, (D - 4) // 2) as pair:
                iteration(2 * pair + 1)
                iteration(2 * pair + 2)
            iteration(D - 3)
            iteration(D - 2)
            iteration(D - 1)
            for s in steps_of(D):
                split_products(D, s)
                if s == STEP[2, TAIL]:
                    add_first(D - 1)
                    pool.wait_ge(added01, D + 1)

        @block.tensor
        def _(pe):
            def group(i, s):
                layer, g, _ = STEPS[s]
                v, p, _ = MIX[layer][g]
                slot, n = slot_of(i, s), tiles_of(layer, g)
                number = isinstance(i, int)
                first, last = g == 0, s in (A_LAST, B_LAST, C_LAST)
                if first:
                    before_it = i + 1 if layer == 0 else i
                    if not (number and before_it < 1):
                        pe.wait_ge(acc_read[layer], before_it)
                    if number and i == (-1 if layer == 0 else 0):
                        pe.wait_ge(w_split[layer], SPLIT_GROUPS[layer])
                        if layer == 0:
                            pe.wait_ge(w0_native, sum(ly == 0 for ly, _ in NATIVE))
                        else:
                            pe.wait_ge(w_in[layer], 16 * W_LOADS[layer])

                def depth(t):
                    return min(PAIR_ROWS, F * SHIFTS - PAIR_ROWS * t) if layer == 0 else min(P, F * H - P * t)

                order = [*range(v + p, n), *range(v + p)]
                for k in order:
                    if k == v + p:
                        pe.wait_ge(z_made, groups_over(i, s))
                    elif k == 0 and v:
                        pe.wait_ge(vect_split, vect_over(i, s))
                    elif k == 0:
                        pe.wait_ge(pool_split, pool_over(i, s))
                    t = GROUP * g + k
                    d = depth(t)
                    if k >= v + p:
                        terms = [(wn[0:d, NATIVE[layer, t], :], z[0:d, slot, k, :])]
                    else:
                        at = SPLIT[layer, t]
                        if layer and t == HALF:
                            terms = [(wh[:, at, :], zl[:, slot, k, :]), (wl[0:H, at, :], zl[0:H, slot, k, :])]
                        else:
                            hi, lo = zh[0:d, zh_at(slot) + k, :], zl[0:d, slot, k, :]
                            terms = [(wh[0:d, at, :], hi), (wl[0:d, at, :], hi), (wh[0:d, at, :], lo)]
                    for m, (w, zz) in enumerate(terms):
                        mm = pe.matmul(acc[layer][:], w, zz, start=first and k == order[0] and m == 0,
                                       stop=last and k == order[-1] and m == len(terms) - 1)
                mm.then_inc(group_used, 1)

            def iteration(i):
                for s in steps_of(i):
                    group(i, s)

            iteration(-1)
            iteration(0)
            with pe.Fori(0, (D - 4) // 2) as pair:
                iteration(2 * pair + 1)
                iteration(2 * pair + 2)
            iteration(D - 3)
            iteration(D - 2)
            iteration(D - 1)
            iteration(D)
            pe.wait_ge(ident_in, 16)
            for layer, total, added, count in ((1, sum01, added01, D + 1), (2, sum2, added2, D + 1)):
                pe.wait_ge(added, count)
                pe.wait_ge(acc_read[layer], D)
                for k in range(B // P):
                    mm = pe.transpose(acc[layer][:, k * L:(k + 1) * L], total[:, k * P:(k + 1) * P], ident[:])
                mm.then_inc(turned, 1)


def kernel(**inputs):
    import numpy as np
    import concourse.bacc as bacc
    from concourse.bass_utils import run_bass_kernel_spmd

    xc = np.ascontiguousarray(inputs["r_x"]).transpose(2, 1, 0)
    xc = np.ascontiguousarray(np.concatenate([xc, xc], axis=1))
    w0 = np.ascontiguousarray(inputs["L0_rec_W0"])
    w0a = np.zeros((P, TILES[0], L), w0.dtype)
    w0b = np.zeros((P, TILES[0], L), w0.dtype)
    for s in range(SHIFTS):
        f = np.arange(F)
        g = (f + s) % F
        at = slice((s % 3) * F, (s % 3 + 1) * F)
        w0a[at, s // 3] = w0[f * F + g]
        if s:
            w0b[at, s // 3] = w0[g * F + f]
    halves = np.stack([xc[:, 0:F:2], xc[:, [*range(1, F, 2), F - 1]]], axis=1)
    arrays = {"x": xc, "x_halves": halves, "w0a": w0a, "w0b": w0b, "w1": inputs["L0_rec_W1"], "w2": inputs["L0_rec_W2"],
              "b": np.stack([inputs[f"L0_rec_b{n}"] for n in range(3)], axis=1),
              "ident": np.eye(P, dtype=np.float32)}
    arrays = {f"in_{k}": np.ascontiguousarray(v) for k, v in arrays.items()}
    nc = bacc.Bacc("TRN2", target_bir_lowering=False, num_devices=1)
    args = [nc.dram_tensor(k, v.shape, mybir.dt.from_np(v.dtype), kind="ExternalInput").ap()
            for k, v in arrays.items()]
    args.append(nc.dram_tensor("out", (B, 2 * L), F32, kind="ExternalOutput").ap())
    cin_kernel(nc, *args)
    return run_bass_kernel_spmd(nc, [arrays], core_ids=[0]).results[0]["out"]
```
